# Optimizing a Trainium2 kernel written in Bass

```python
import numpy as np
import jax
import jax.numpy as jnp

def _softmax(x, axis=-1):
    return jax.nn.softmax(x, axis=axis)

def _gelu(x):
    return jax.nn.gelu(x, approximate=True)

def _silu(x):
    return jax.nn.silu(x)

def _sigmoid(x):
    return jax.nn.sigmoid(x)

def _layernorm(x, axis=-1, eps=1e-05):
    m = jnp.mean(x, axis=axis, keepdims=True)
    v = jnp.var(x, axis=axis, keepdims=True)
    return (x - m) / jnp.sqrt(v + eps)

def _scatter_add(tgt, idx, src, axis=0):
    return tgt.at[idx].add(src)

def _segment_sum(src, seg, n):
    return jax.ops.segment_sum(src, seg, n)
kernel_name = 'mk_dlrm_tower_d1_rec_r8_e1b013'

def setup_inputs(seed: int=0):
    np.random.seed(seed)
    _w = jnp.asarray

    def _rec_inputs():
        import jax
        import jax.numpy as jnp
        _tk = jax.random.key(seed)
        ids = jnp.stack([jax.random.randint(jax.random.fold_in(_tk, 200 + f), (2048,), 0, v, jnp.int32) for f, v in enumerate([125000, 1000, 12500, 1250, 1000, 1000, 12500, 1250, 1000, 1250, 1000, 12500, 12500, 12500, 1000, 1000, 12500, 1000, 12500, 1000, 1000, 1250, 1250, 1250, 12500, 1250])], axis=1)
        tbl_0 = 0.05 * jax.random.normal(jax.random.fold_in(_tk, 500 + 0), (125000, 128), jnp.float32)
        tbl_1 = 0.05 * jax.random.normal(jax.random.fold_in(_tk, 500 + 1), (1000, 128), jnp.float32)
        tbl_2 = 0.05 * jax.random.normal(jax.random.fold_in(_tk, 500 + 2), (12500, 128), jnp.float32)
        tbl_3 = 0.05 * jax.random.normal(jax.random.fold_in(_tk, 500 + 3), (1250, 128), jnp.float32)
        tbl_4 = 0.05 * jax.random.normal(jax.random.fold_in(_tk, 500 + 4), (1000, 128), jnp.float32)
        tbl_5 = 0.05 * jax.random.normal(jax.random.fold_in(_tk, 500 + 5), (1000, 128), jnp.float32)
        tbl_6 = 0.05 * jax.random.normal(jax.random.fold_in(_tk, 500 + 6), (12500, 128), jnp.float32)
        tbl_7 = 0.05 * jax.random.normal(jax.random.fold_in(_tk, 500 + 7), (1250, 128), jnp.float32)
        tbl_8 = 0.05 * jax.random.normal(jax.random.fold_in(_tk, 500 + 8), (1000, 128), jnp.float32)
        tbl_9 = 0.05 * jax.random.normal(jax.random.fold_in(_tk, 500 + 9), (1250, 128), jnp.float32)
        tbl_10 = 0.05 * jax.random.normal(jax.random.fold_in(_tk, 500 + 10), (1000, 128), jnp.float32)
        tbl_11 = 0.05 * jax.random.normal(jax.random.fold_in(_tk, 500 + 11), (12500, 128), jnp.float32)
        tbl_12 = 0.05 * jax.random.normal(jax.random.fold_in(_tk, 500 + 12), (12500, 128), jnp.float32)
        tbl_13 = 0.05 * jax.random.normal(jax.random.fold_in(_tk, 500 + 13), (12500, 128), jnp.float32)
        tbl_14 = 0.05 * jax.random.normal(jax.random.fold_in(_tk, 500 + 14), (1000, 128), jnp.float32)
        tbl_15 = 0.05 * jax.random.normal(jax.random.fold_in(_tk, 500 + 15), (1000, 128), jnp.float32)
        tbl_16 = 0.05 * jax.random.normal(jax.random.fold_in(_tk, 500 + 16), (12500, 128), jnp.float32)
        tbl_17 = 0.05 * jax.random.normal(jax.random.fold_in(_tk, 500 + 17), (1000, 128), jnp.float32)
        tbl_18 = 0.05 * jax.random.normal(jax.random.fold_in(_tk, 500 + 18), (12500, 128), jnp.float32)
        tbl_19 = 0.05 * jax.random.normal(jax.random.fold_in(_tk, 500 + 19), (1000, 128), jnp.float32)
        tbl_20 = 0.05 * jax.random.normal(jax.random.fold_in(_tk, 500 + 20), (1000, 128), jnp.float32)
        tbl_21 = 0.05 * jax.random.normal(jax.random.fold_in(_tk, 500 + 21), (1250, 128), jnp.float32)
        tbl_22 = 0.05 * jax.random.normal(jax.random.fold_in(_tk, 500 + 22), (1250, 128), jnp.float32)
        tbl_23 = 0.05 * jax.random.normal(jax.random.fold_in(_tk, 500 + 23), (1250, 128), jnp.float32)
        tbl_24 = 0.05 * jax.random.normal(jax.random.fold_in(_tk, 500 + 24), (12500, 128), jnp.float32)
        tbl_25 = 0.05 * jax.random.normal(jax.random.fold_in(_tk, 500 + 25), (1250, 128), jnp.float32)
        _rk = jax.random.fold_in(_tk, 7)
        r_dense_features = -0.000520686 + 1.00062 * jax.random.normal(jax.random.fold_in(_rk, 101), (2048, 128), jnp.float32)
        W_top1 = 0.0405887 * jax.random.normal(jax.random.fold_in(_tk, 801), (607, 512), jnp.float32)
        W_top2 = 0.0441942 * jax.random.normal(jax.random.fold_in(_tk, 802), (512, 256), jnp.float32)
        W_top3 = 0.0625 * jax.random.normal(jax.random.fold_in(_tk, 803), (256, 1), jnp.float32)
        b_top1 = jnp.zeros((512,), jnp.float32)
        b_top2 = jnp.zeros((256,), jnp.float32)
        return (r_dense_features, ids, tbl_0, tbl_1, tbl_2, tbl_3, tbl_4, tbl_5, tbl_6, tbl_7, tbl_8, tbl_9, tbl_10, tbl_11, tbl_12, tbl_13, tbl_14, tbl_15, tbl_16, tbl_17, tbl_18, tbl_19, tbl_20, tbl_21, tbl_22, tbl_23, tbl_24, tbl_25, W_top1, b_top1, W_top2, b_top2, W_top3)
    r_dense_features, ids, tbl_0, tbl_1, tbl_2, tbl_3, tbl_4, tbl_5, tbl_6, tbl_7, tbl_8, tbl_9, tbl_10, tbl_11, tbl_12, tbl_13, tbl_14, tbl_15, tbl_16, tbl_17, tbl_18, tbl_19, tbl_20, tbl_21, tbl_22, tbl_23, tbl_24, tbl_25, W_top1, b_top1, W_top2, b_top2, W_top3 = _rec_inputs()

    def _L0_rec_setup():
        import jax, jax.numpy as jnp
        import numpy as np
        NUM_SPARSE = 26
        EMBED_DIM = 128
        BATCH = 2048
        key = jax.random.key(seed)
        k1, k2 = jax.random.split(key)
        dense_features = jax.random.normal(k1, (BATCH, EMBED_DIM), dtype=jnp.float32)
        sparse_features = jax.random.normal(k2, (BATCH, NUM_SPARSE, EMBED_DIM), dtype=jnp.float32)
        return {'dense_features': dense_features, 'sparse_features': sparse_features}
    _L0_rec_all = _L0_rec_setup()
    _L0_rec_in = {k: v for k, v in _L0_rec_all.items() if k in ()}
    del _L0_rec_all
    return {'r_dense_features': r_dense_features, 'ids': ids, 'tbl_0': tbl_0, 'tbl_1': tbl_1, 'tbl_2': tbl_2, 'tbl_3': tbl_3, 'tbl_4': tbl_4, 'tbl_5': tbl_5, 'tbl_6': tbl_6, 'tbl_7': tbl_7, 'tbl_8': tbl_8, 'tbl_9': tbl_9, 'tbl_10': tbl_10, 'tbl_11': tbl_11, 'tbl_12': tbl_12, 'tbl_13': tbl_13, 'tbl_14': tbl_14, 'tbl_15': tbl_15, 'tbl_16': tbl_16, 'tbl_17': tbl_17, 'tbl_18': tbl_18, 'tbl_19': tbl_19, 'tbl_20': tbl_20, 'tbl_21': tbl_21, 'tbl_22': tbl_22, 'tbl_23': tbl_23, 'tbl_24': tbl_24, 'tbl_25': tbl_25, 'W_top1': W_top1, 'b_top1': b_top1, 'W_top2': W_top2, 'b_top2': b_top2, 'W_top3': W_top3}

def reference(r_dense_features, ids, tbl_0, tbl_1, tbl_2, tbl_3, tbl_4, tbl_5, tbl_6, tbl_7, tbl_8, tbl_9, tbl_10, tbl_11, tbl_12, tbl_13, tbl_14, tbl_15, tbl_16, tbl_17, tbl_18, tbl_19, tbl_20, tbl_21, tbl_22, tbl_23, tbl_24, tbl_25, W_top1, b_top1, W_top2, b_top2, W_top3):
    import jax
    import jax.numpy as jnp

    def _L0_rec_ref(dense_features, sparse_features):
        import jax, jax.numpy as jnp
        import numpy as np
        NUM_SPARSE = 26
        EMBED_DIM = 128
        BATCH = 2048
        F = NUM_SPARSE + 1
        combined = jnp.concatenate([dense_features[:, None, :], sparse_features], axis=1)
        interactions = jnp.einsum('bfd,bgd->bfg', combined, combined)
        iu, ju = jnp.triu_indices(F, k=1)
        interactions_flat = interactions[:, iu, ju]
        return jnp.concatenate([dense_features, interactions_flat], axis=1)
    e = jnp.stack([tbl_0[ids[:, 0]], tbl_1[ids[:, 1]], tbl_2[ids[:, 2]], tbl_3[ids[:, 3]], tbl_4[ids[:, 4]], tbl_5[ids[:, 5]], tbl_6[ids[:, 6]], tbl_7[ids[:, 7]], tbl_8[ids[:, 8]], tbl_9[ids[:, 9]], tbl_10[ids[:, 10]], tbl_11[ids[:, 11]], tbl_12[ids[:, 12]], tbl_13[ids[:, 13]], tbl_14[ids[:, 14]], tbl_15[ids[:, 15]], tbl_16[ids[:, 16]], tbl_17[ids[:, 17]], tbl_18[ids[:, 18]], tbl_19[ids[:, 19]], tbl_20[ids[:, 20]], tbl_21[ids[:, 21]], tbl_22[ids[:, 22]], tbl_23[ids[:, 23]], tbl_24[ids[:, 24]], tbl_25[ids[:, 25]]], axis=1)
    z = _L0_rec_ref(r_dense_features, e)
    z = z.reshape(z.shape[0], -1)
    h = jnp.concatenate([z, r_dense_features], axis=1)
    h = jnp.maximum(h @ W_top1 + b_top1, 0.0)
    h = jnp.maximum(h @ W_top2 + b_top2, 0.0)
    y = h @ W_top3
    return y

_drawn_inputs = setup_inputs


def setup_inputs(seed=0):
    import zlib

    import numpy as np

    out = dict(_drawn_inputs(seed))
    spreads = {'b_top1': (0.0, 0.1), 'b_top2': (0.0, 0.1)}
    factors = {}
    for name, (base, spread) in spreads.items():
        noise = np.random.default_rng([zlib.crc32(name.encode()), seed]).standard_normal(out[name].shape)
        drawn = base * np.exp(spread * noise) if base else spread * noise
        out[name] = jnp.asarray(drawn.astype(out[name].dtype))
    for name, factor in factors.items():
        out[name] = (out[name] * factor).astype(out[name].dtype)
    return out
```

```python
import concourse.bass as bass
from concourse import mybir
from contextlib import ExitStack

NUM_TABLES = 26
FEATURES = NUM_TABLES + 1
DIM = 128
P = 128
BATCH = 2048
CHUNK = 256
CHUNKS = BATCH // CHUNK
TILES_PER_CHUNK = CHUNK // P
HIDDEN1, HIDDEN2 = 512, 256
ROWS = [125000, 1000, 12500, 1250, 1000, 1000, 12500, 1250, 1000, 1250, 1000, 12500, 12500, 12500,
        1000, 1000, 12500, 1000, 12500, 1000, 1000, 1250, 1250, 1250, 12500, 1250]

PICKED = [1, 4, 5, 8]
GATHERED = [f for f in range(NUM_TABLES) if f not in PICKED]
PICK_ROWS = 1000
PICK_PARTS = 125
PICK_PER_PART = PICK_ROWS // PICK_PARTS
SPLITS = 3

ORDER = [0] + [1 + f for f in GATHERED] + [1 + f for f in PICKED]
MOVED = 1 + len(GATHERED)
POSITIONS = 32
GROUP = 4
GROUPS = [list(range(a, min(a + GROUP, MOVED))) for a in range(0, MOVED, GROUP)]
BLOCKS = 4
SLOTS = 7
SECONDS = FEATURES - 1
QUADS = 8
GRAM_GROUPS = P // (BLOCKS * QUADS)
L1_BLOCKS, L2_BLOCKS = HIDDEN1 // P, HIDDEN2 // P


def slots_of(j):
    return min(SLOTS, SECONDS - SLOTS * j)


def build(nc, dense, ids, ids_rows, tables, w_pairs, w_dense, b1, w2, b2, w3, identity, row_ids, out):
    fp32, bf16, fp16, i32 = mybir.dt.float32, mybir.dt.bfloat16, mybir.dt.float16, mybir.dt.int32
    ALU = mybir.AluOpType
    ACT = mybir.ActivationFunctionType
    N = len(PICKED)
    NG = len(GROUPS)
    assert NG % 2 == 0, "each bank of transposes serves every second group"
    HALF = NG // 2

    ctx = ExitStack()
    with ctx:
        def sb(name, shape, dt):
            return ctx.enter_context(nc.sbuf_tensor(name, shape, dt))

        def sem(name):
            return ctx.enter_context(nc.semaphore(name))

        idx = sb("idx", [P, 2, NUM_TABLES], i32)
        rows = sb("rows", [P, 2, MOVED, DIM], fp32)
        xt = sb("xt", [P, 2, P, POSITIONS], fp32)
        pairs = sb("pairs", [P, SLOTS, CHUNK], fp32)
        dense_t = sb("dense_t", [P, CHUNK], fp32)
        h1 = sb("h1", [P, L1_BLOCKS, CHUNK], fp32)
        h2 = sb("h2", [P, L2_BLOCKS, CHUNK], fp32)
        y = sb("y", [1, BATCH], fp32)
        wp = sb("wp", [P, SLOTS, HIDDEN1], fp32)
        wd = sb("wd", [P, HIDDEN1], fp32)
        wd2 = sb("wd2", [P, 2, HIDDEN1], fp32)
        w2s = sb("w2s", [P, L1_BLOCKS, HIDDEN2], fp32)
        w3s = sb("w3s", [P, L2_BLOCKS], fp32)
        b1s = sb("b1s", [P, L1_BLOCKS], fp32)
        b2s = sb("b2s", [P, L2_BLOCKS], fp32)
        ident = sb("ident", [P, P], fp32)
        row_id = sb("row_id", [PICK_PARTS, PICK_PER_PART], fp32)
        tab = sb("tab", [PICK_PARTS, N, PICK_PER_PART * DIM], fp32)
        rest = sb("rest", [PICK_PARTS, 2, PICK_PER_PART * DIM], fp32)
        tabs = sb("tabs", [PICK_PARTS, N, SPLITS, PICK_PER_PART, DIM], bf16)
        ids32 = sb("ids32", [PICK_PARTS, N, CHUNK], i32)
        ids16 = sb("ids16", [PICK_PARTS, N, CHUNK], fp16)
        onehot = sb("onehot", [PICK_PARTS, N, PICK_PER_PART, CHUNK], bf16)

        p_tr = ctx.enter_context(nc.psum_tensor("p_tr", [P, 2, GROUP, P], fp32))
        p_gram = ctx.enter_context(nc.psum_tensor("p_gram", [P, 2, QUADS, P], fp32))
        p_out = ctx.enter_context(nc.psum_tensor("p_out", [P, 2, 512], fp32))

        idx_loaded = [sem(f"idx_loaded{c}") for c in range(2)]
        dense_loaded = [sem(f"dense_loaded{c}") for c in range(2)]
        rows_free = sem("rows_free")
        gathered = [[sem(f"gathered{c}_{g}") for g in range(NG)] for c in range(2)]
        ids_loaded = sem("ids_loaded")
        ids_taken = sem("ids_taken")
        ident_loaded = sem("ident_loaded")
        row_id_loaded = sem("row_id_loaded")
        tab_loaded = [sem(f"tab_loaded{u}") for u in range(N)]
        weights_loaded = sem("weights_loaded")
        wd2_loaded = sem("wd2_loaded")
        wd_ready = sem("wd_ready")
        zeroed = sem("zeroed")
        high_cut = sem("high_cut")
        rest1_ready = sem("rest1_ready")
        middle_cut = sem("middle_cut")
        tabs_ready = sem("tabs_ready")
        onehot_ready = sem("onehot_ready")
        transposed = [sem(f"transposed{b}") for b in range(2)]
        tr_taken = [sem(f"tr_taken{b}") for b in range(2)]
        dense_kept = sem("dense_kept")
        gram_ready = sem("gram_ready")
        gram_taken = {"act": sem("gram_taken_act"), "dve": sem("gram_taken_dve")}
        out_ready = [sem(f"out_ready{b}") for b in range(2)]
        out_taken = [sem(f"out_taken{b}") for b in range(2)]
        y_written = sem("y_written")

        def wait(eng, s, count):
            if not isinstance(count, int) or count > 0:
                eng.wait_ge(s, count)

        def tr_count(i, c, g):
            return (2 * i + c) * HALF + g // 2

        def gram_count(i, c, k):
            return (TILES_PER_CHUNK * i + c) * GRAM_GROUPS + k

        PICK_USES = [(N + 1) // 2, N // 2]
        L1_USES = L1_BLOCKS // 2
        LAYER_USES = [L1_USES + 1 + 1, L1_USES + 1]

        def out_count(i, b, stage, n=0):
            before = {"pick": 0, "l1": PICK_USES[b], "l2": PICK_USES[b] + L1_USES,
                      "l3": PICK_USES[b] + L1_USES + 1}[stage]
            steps = 0 if isinstance(i, int) and i == 0 else i * PICK_USES[b] + (i - 1) * LAYER_USES[b]
            if isinstance(i, int) and i == CHUNKS and stage != "pick":
                before -= PICK_USES[b]
            return steps + before + n

        block = ctx.enter_context(nc.Block())

        @block.sync
        def _(sp):
            def load_tile(i, c):
                if not (isinstance(i, int) and i == 0):
                    wait(sp, transposed[0], tr_count(i - 1, c, NG))
                    wait(sp, transposed[1], tr_count(i - 1, c, NG))
                at = i * CHUNK + c * P
                sp.dma_start(idx[:, c, :], ids[bass.ds(at, P), :]).then_inc(idx_loaded[c], 16)
                sp.dma_start(rows[:, c, 0, :], dense[bass.ds(at, P), :]).then_inc(dense_loaded[c], 16)

            def load_ids(i):
                if not (isinstance(i, int) and i == 0):
                    wait(sp, ids_taken, i)
                for u in range(N):
                    sp.dma_start(ids32[:, u, :],
                                 ids_rows[PICKED[u]:PICKED[u] + 1, bass.ds(i * CHUNK, CHUNK)]
                                 .to_broadcast([PICK_PARTS, CHUNK])).then_inc(ids_loaded, 16)

            load_tile(0, 0)
            sp.dma_start(ident[:], identity).then_inc(ident_loaded, 16)
            load_tile(0, 1)
            sp.dma_start(row_id[:], row_ids).then_inc(row_id_loaded, 16)
            for u in range(N):
                sp.dma_start(tab[:, u, :], tables[PICKED[u]].rearrange("(p k) d -> p (k d)", k=PICK_PER_PART)
                             ).then_inc(tab_loaded[u], 16)
                if u == 0:
                    load_ids(0)
            with sp.Fori(1, CHUNKS) as i:
                load_ids(i)
                for c in range(TILES_PER_CHUNK):
                    load_tile(i, c)
            wait(sp, out_taken[0], out_count(CHUNKS, 0, "l3", 1))
            sp.dma_start(out, y[:]).then_inc(y_written, 16)
            sp.wait_ge(y_written, 16)

        @block.gpsimd
        def _(pool):
            def gather_tile(i, c):
                wait(pool, idx_loaded[c], 16 * (i + 1))
                for g, group in enumerate(GROUPS):
                    if not (isinstance(i, int) and i == 0):
                        wait(pool, transposed[g % 2], tr_count(i - 1, c, g) + 1)
                        pool.sem_inc(rows_free, 1)
                    for pos in group:
                        if pos:
                            f = GATHERED[pos - 1]
                            pool.indirect_dma_start(
                                rows[:, c, pos, :], None, tables[f],
                                bass.IndirectOffsetOnAxis(idx[:, c, f:f + 1], 0)).then_inc(gathered[c][g], 16)

            for c in range(TILES_PER_CHUNK):
                gather_tile(0, c)
            with pool.Fori(1, CHUNKS) as i:
                for c in range(TILES_PER_CHUNK):
                    gather_tile(i, c)

        @block.tensor
        def _(pe):
            def claim(i, b, stage, n=0):
                wait(pe, out_taken[b], out_count(i, b, stage, n))

            def pick(i):
                for u in range(N):
                    claim(i, u % 2, "pick", u // 2)
                    wait(pe, onehot_ready, N * i + u + 1)
                    for k in range(PICK_PER_PART):
                        for s in range(SPLITS):
                            last = nc.tensor.matmul(p_out[:, u % 2, 0:CHUNK], tabs[:, u, s, k, :],
                                                    onehot[:, u, k, :], start=(k == 0 and s == 0),
                                                    stop=(k == PICK_PER_PART - 1 and s == SPLITS - 1))
                    last.then_inc(out_ready[u % 2], 1)

            def transpose_tile(i, c):
                for g, group in enumerate(GROUPS):
                    if g == 0:
                        wait(pe, dense_loaded[c], 16 * (i + 1))
                    n_dma = len([pos for pos in group if pos])
                    wait(pe, gathered[c][g], 16 * n_dma * (i + 1))
                    wait(pe, tr_taken[g % 2], tr_count(i, c, g))
                    for q, pos in enumerate(group):
                        last = nc.tensor.transpose(p_tr[:, g % 2, q, :], rows[:, c, pos, :], ident[:])
                    last.then_inc(transposed[g % 2], 1)

            def gram_tile(i, c):
                if c == 0:
                    for b in range(2):
                        wait(pe, out_taken[b], out_count(i, b, "l1"))
                for b in range(2):
                    wait(pe, tr_taken[b], tr_count(i, c, NG))
                x = xt[:, c, :, :].rearrange("p (k q s) f -> p k q s f", s=BLOCKS, q=QUADS)
                for k in range(GRAM_GROUPS):
                    for taken in gram_taken.values():
                        wait(pe, taken, gram_count(i, c, k - 1))
                    for q in range(QUADS):
                        last = nc.tensor.matmul(p_gram[:, k % 2, q, 0:BLOCKS * SECONDS], x[:, k, q, :, :].rearrange("p s f -> p (s f)"),
                                                x[:, k, q, :, 1:1 + SECONDS], start=True, stop=True)
                    last.then_inc(gram_ready, 1)

            def layer1(i):
                for taken in gram_taken.values():
                    wait(pe, taken, gram_count(i, 0, 0))
                wait(pe, dense_kept, TILES_PER_CHUNK * i)
                for m in range(L1_BLOCKS):
                    claim(i, m % 2, "l1", m // 2)
                    cols = slice(m * P, (m + 1) * P)
                    nc.tensor.matmul(p_out[:, m % 2, 0:CHUNK], wd[:, cols], dense_t[:], start=True, stop=False)
                    for k in range(SLOTS):
                        last = nc.tensor.matmul(p_out[:, m % 2, 0:CHUNK], wp[:, k, cols], pairs[:, k, :],
                                                start=False, stop=(k == SLOTS - 1))
                    last.then_inc(out_ready[m % 2], 1)

            def layer2(i):
                for b in range(2):
                    wait(pe, out_taken[b], out_count(i, b, "l2"))
                for m in range(L2_BLOCKS):
                    for k in range(L1_BLOCKS):
                        last = nc.tensor.matmul(p_out[:, m, 0:CHUNK], w2s[:, k, m * P:(m + 1) * P], h1[:, k, :],
                                                start=(k == 0), stop=(k == L1_BLOCKS - 1))
                    last.then_inc(out_ready[m], 1)

            def layer3(i):
                for b in range(2):
                    wait(pe, out_taken[b], out_count(i, b, "l3"))
                for k in range(L2_BLOCKS):
                    last = nc.tensor.matmul(p_out[0:1, 0, 0:CHUNK], w3s[:, k:k + 1], h2[:, k, :],
                                            start=(k == 0), stop=(k == L2_BLOCKS - 1))
                last.then_inc(out_ready[0], 1)

            def step(i, layers=True):
                pick(i)
                transpose_tile(i, 0)
                if layers:
                    layer1(i)
                gram_tile(i, 0)
                transpose_tile(i, 1)
                if layers:
                    layer2(i)
                gram_tile(i, 1)
                if layers:
                    layer3(i)

            wait(pe, ident_loaded, 16)
            wait(pe, tabs_ready, N)
            wait(pe, zeroed, 2)
            step(0, layers=False)
            wait(pe, weights_loaded, 5 * 16)
            wait(pe, wd_ready, 1)
            with pe.Fori(1, CHUNKS) as i:
                step(i)
            layer1(CHUNKS)
            layer2(CHUNKS)
            layer3(CHUNKS)

        def copy_group(copy, c, g, done):
            group = GROUPS[g]
            src = p_tr[:, g % 2, 0:len(group), :].rearrange("p f s -> p s f")
            copy(xt[:, c, :, group[0]:group[-1] + 1], src).then_inc(done, 1)

        def copy_gram(copy, c, k, blocks, done):
            x = pairs[:, :, c * P:(c + 1) * P].rearrange("p g (k q s) -> p g k s q", s=BLOCKS, q=QUADS)
            for s in blocks:
                for j in range(BLOCKS):
                    n = slots_of(j)
                    at = s * SECONDS + SLOTS * j
                    last = copy(x[32 * j:32 * j + 32, 0:n, k, s, :],
                                p_gram[32 * s:32 * s + 32, k % 2, :, at:at + n].rearrange("p q g -> p g q"))
            last.then_inc(done, 1)

        @block.scalar
        def _(act):
            copy = nc.scalar.copy
            act.dma_start(wd2[:], w_dense).then_inc(wd2_loaded, 16)
            act.dma_start(b1s[:], b1).then_inc(weights_loaded, 16)
            act.dma_start(b2s[:], b2).then_inc(weights_loaded, 16)
            act.dma_start(w3s[:], w3).then_inc(weights_loaded, 16)
            for u in range(N):
                act.wait_ge(tab_loaded[u], 16)
                copy(tabs[:, u, 0, :, :].rearrange("p k d -> p (k d)"), tab[:, u, :]).then_inc(high_cut, 1)
                act.wait_ge(rest1_ready, u + 1)
                copy(tabs[:, u, 1, :, :].rearrange("p k d -> p (k d)"), rest[:, u % 2, :]).then_inc(middle_cut, 1)
            act.dma_start(w2s[:], w2).then_inc(weights_loaded, 16)
            act.dma_start(wp[:], w_pairs).then_inc(weights_loaded, 16)

            def take_picked(i):
                for u in range(N):
                    b = u % 2
                    act.wait_ge(out_ready[b], out_count(i, b, "pick", u // 2 + 1))
                    copy(xt[:, :, :, MOVED + u],
                         p_out[:, b, 0:CHUNK].rearrange("p (c s) -> p c s", c=2)).then_inc(out_taken[b], 1)

            def take_transposes(i, c):
                for g in range(1, NG, 2):
                    act.wait_ge(transposed[1], tr_count(i, c, g) + 1)
                    copy_group(copy, c, g, tr_taken[1])

            def take_gram(i, c):
                act.wait_ge(tr_taken[0], tr_count(i, c, 0) + 1)
                copy(dense_t[:, c * P:(c + 1) * P], xt[:, c, :, 0]).then_inc(dense_kept, 1)
                for k in range(GRAM_GROUPS):
                    act.wait_ge(gram_ready, gram_count(i, c, k + 1))
                    copy_gram(copy, c, k, (0, 1), gram_taken["act"])

            def take_layer1(i):
                for m in range(L1_BLOCKS):
                    act.wait_ge(out_ready[m % 2], out_count(i, m % 2, "l1", m // 2 + 1))
                    nc.scalar.activation(h1[:, m, :], p_out[:, m % 2, 0:CHUNK], ACT.Relu,
                                         bias=b1s[:, m:m + 1]).then_inc(out_taken[m % 2], 1)

            def take_layer2(i):
                for m in range(L2_BLOCKS):
                    act.wait_ge(out_ready[m], out_count(i, m, "l2", 1))
                    nc.scalar.activation(h2[:, m, :], p_out[:, m, 0:CHUNK], ACT.Relu,
                                         bias=b2s[:, m:m + 1]).then_inc(out_taken[m], 1)

            def take_layer3(i):
                act.wait_ge(out_ready[0], out_count(i, 0, "l3", 1))
                copy(y[:, bass.ds((i - 1) * CHUNK, CHUNK)], p_out[0:1, 0, 0:CHUNK]).then_inc(out_taken[0], 1)

            def step(i, layers=True):
                take_picked(i)
                take_transposes(i, 0)
                if layers:
                    take_layer1(i)
                take_gram(i, 0)
                take_transposes(i, 1)
                if layers:
                    take_layer2(i)
                take_gram(i, 1)
                if layers:
                    take_layer3(i)

            act.wait_ge(zeroed, 2)
            step(0, layers=False)
            act.wait_ge(weights_loaded, 5 * 16)
            with act.Fori(1, CHUNKS) as i:
                step(i)
            take_layer1(CHUNKS)
            take_layer2(CHUNKS)
            take_layer3(CHUNKS)

        @block.vector
        def _(dve):
            copy = nc.vector.tensor_copy

            def make_onehots(i):
                dve.wait_ge(ids_loaded, 16 * N * (i + 1))
                copy(ids16[:], ids32[:]).then_inc(ids_taken, 1)
                dve.wait_ge(ids_taken, i + 1)
                for u in range(N):
                    if not (isinstance(i, int) and i == 0):
                        dve.wait_ge(out_ready[u % 2], out_count(i - 1, u % 2, "pick", u // 2 + 1))
                    for k in range(PICK_PER_PART):
                        last = nc.vector.tensor_scalar(onehot[:, u, k, :], ids16[:, u, :], row_id[:, k:k + 1],
                                                       None, ALU.is_equal)
                    last.then_inc(onehot_ready, 1)

            def take_transposes(i, c):
                wait(dve, dense_kept, TILES_PER_CHUNK * i + c - 1)
                for g in range(0, NG, 2):
                    dve.wait_ge(transposed[0], tr_count(i, c, g) + 1)
                    copy_group(copy, c, g, tr_taken[0])

            def take_gram(i, c):
                for k in range(GRAM_GROUPS):
                    dve.wait_ge(gram_ready, gram_count(i, c, k + 1))
                    copy_gram(copy, c, k, (2, 3), gram_taken["dve"])

            def step(i, first=False, last=False):
                take_transposes(i, 0)
                if not last:
                    make_onehots(i + 1)
                if not first:
                    dve.wait_ge(out_ready[1], out_count(i, 1, "l1", L1_USES))
                take_gram(i, 0)
                take_transposes(i, 1)
                take_gram(i, 1)

            nc.vector.memset(xt[:], 0.0).then_inc(zeroed, 1)
            nc.vector.memset(pairs[:], 0.0).then_inc(zeroed, 1)
            for u in range(N):
                flat = [tabs[:, u, s, :, :].rearrange("p k d -> p (k d)") for s in range(SPLITS)]
                dve.wait_ge(high_cut, u + 1)
                if u >= 2:
                    dve.wait_ge(tabs_ready, u - 1)
                nc.vector.tensor_tensor(rest[:, u % 2, :], tab[:, u, :], flat[0], ALU.subtract
                                        ).then_inc(rest1_ready, 1)
                dve.wait_ge(rest1_ready, u + 1)
                dve.wait_ge(middle_cut, u + 1)
                nc.vector.tensor_tensor(flat[2], rest[:, u % 2, :], flat[1], ALU.subtract).then_inc(tabs_ready, 1)
            dve.wait_ge(row_id_loaded, 16)
            make_onehots(0)
            dve.wait_ge(wd2_loaded, 16)
            nc.vector.tensor_tensor(wd[:], wd2[:, 0, :], wd2[:, 1, :], ALU.add).then_inc(wd_ready, 1)
            step(0, first=True)
            with dve.Fori(1, CHUNKS - 1) as i:
                step(i)
            step(CHUNKS - 1, last=True)


def kernel(**inputs):
    import numpy as np
    import concourse.bacc as bacc
    from concourse import mybir as _mybir
    from concourse.bass_utils import run_bass_kernel_spmd

    nc = bacc.Bacc("TRN2", target_bir_lowering=False, num_devices=1)
    arrays = {}

    def give(name, a):
        a = np.ascontiguousarray(a)
        arrays[name] = a
        return nc.dram_tensor(name, a.shape, _mybir.dt.from_np(a.dtype), kind="ExternalInput").ap()

    ids = np.asarray(inputs["ids"])
    w1 = np.asarray(inputs["W_top1"])
    n_pairs = FEATURES * (FEATURES - 1) // 2
    w_pairs = np.zeros((BLOCKS, 32, SLOTS, HIDDEN1), w1.dtype)
    for b in range(1, FEATURES):
        j, slot = (b - 1) // SLOTS, (b - 1) % SLOTS
        for a in range(b):
            f, g = sorted((ORDER[a], ORDER[b]))
            w_pairs[j, a, slot] = w1[DIM + f * FEATURES - f * (f + 1) // 2 + g - f - 1]
    w_dense = np.stack([w1[:DIM], w1[DIM + n_pairs:]], axis=1)
    out = nc.dram_tensor("y_out", (BATCH, 1), _mybir.dt.from_np(w1.dtype), kind="ExternalOutput").ap()
    build(
        nc,
        dense=give("dense", inputs["r_dense_features"]),
        ids=give("ids", ids),
        ids_rows=give("ids_rows", ids.T),
        tables=[give(f"tbl_{f}", inputs[f"tbl_{f}"]) for f in range(NUM_TABLES)],
        w_pairs=give("w_pairs", w_pairs.reshape(P, SLOTS, HIDDEN1)),
        w_dense=give("w_dense", w_dense),
        b1=give("b1", np.asarray(inputs["b_top1"]).reshape(L1_BLOCKS, P).T),
        w2=give("w2", np.asarray(inputs["W_top2"]).reshape(L1_BLOCKS, P, HIDDEN2).transpose(1, 0, 2)),
        b2=give("b2", np.asarray(inputs["b_top2"]).reshape(L2_BLOCKS, P).T),
        w3=give("w3", np.asarray(inputs["W_top3"]).reshape(L2_BLOCKS, P).T),
        identity=give("identity", np.eye(P, dtype=np.float32)),
        row_ids=give("row_ids", np.arange(PICK_ROWS, dtype=np.float32).reshape(PICK_PARTS, PICK_PER_PART)),
        out=out.rearrange("b o -> o b"),
    )
    r = run_bass_kernel_spmd(nc, [arrays], core_ids=[0])
    return r.results[0]["y_out"]
```

```python
import concourse.bass as bass
from concourse import mybir
from contextlib import ExitStack

NUM_TABLES = 26
FEATURES = NUM_TABLES + 1
DIM = 128
P = 128
BATCH = 2048
CHUNK = 256
CHUNKS = BATCH // CHUNK
TILES_PER_CHUNK = CHUNK // P
HIDDEN1, HIDDEN2 = 512, 256
ROWS = [125000, 1000, 12500, 1250, 1000, 1000, 12500, 1250, 1000, 1250, 1000, 12500, 12500, 12500,
        1000, 1000, 12500, 1000, 12500, 1000, 1000, 1250, 1250, 1250, 12500, 1250]

PICKED = [1, 4, 5, 8, 10, 14]
GATHERED = [f for f in range(NUM_TABLES) if f not in PICKED]
PICK_ROWS = 1000
PICK_PARTS = 125
PICK_PER_PART = PICK_ROWS // PICK_PARTS
ONEHOTS = len(PICKED) // 2

ORDER = [0] + [1 + f for f in GATHERED] + [1 + f for f in PICKED]
MOVED = 1 + len(GATHERED)
POSITIONS = 32
GROUP = 4
GROUPS = [list(range(a, min(a + GROUP, MOVED))) for a in range(0, MOVED, GROUP)]
BLOCKS = 4
SLOTS = 7
SECONDS = FEATURES - 1
QUADS = 8
GRAM_GROUPS = P // (BLOCKS * QUADS)
L1_BLOCKS, L2_BLOCKS = HIDDEN1 // P, HIDDEN2 // P


def slots_of(j):
    return min(SLOTS, SECONDS - SLOTS * j)


def build(nc, dense, ids, ids_rows, tables, w_pairs, w_dense, b1, w2, b2, w3, identity, row_ids, out):
    fp32, fp32r, i32 = mybir.dt.float32, mybir.dt.float32r, mybir.dt.int32
    ALU = mybir.AluOpType
    ACT = mybir.ActivationFunctionType
    N = len(PICKED)
    NG = len(GROUPS)
    assert NG % 2 == 0, "each bank of transposes serves every second group"
    HALF = NG // 2

    ctx = ExitStack()
    with ctx:
        def sb(name, shape, dt):
            return ctx.enter_context(nc.sbuf_tensor(name, shape, dt))

        def sem(name):
            return ctx.enter_context(nc.semaphore(name))

        idx = sb("idx", [P, 2, NUM_TABLES], i32)
        rows = sb("rows", [P, 2, MOVED, DIM], fp32)
        xt = sb("xt", [P, 2, P, POSITIONS], fp32)
        pairs = sb("pairs", [P, SLOTS, CHUNK], fp32)
        pairs_high = sb("pairs_high", [P, SLOTS, CHUNK], fp32r)
        pairs_low = sb("pairs_low", [P, SLOTS, CHUNK], fp32r)
        dense_high = sb("dense_high", [P, CHUNK], fp32r)
        dense_low = sb("dense_low", [P, CHUNK], fp32r)
        h1 = sb("h1", [P, L1_BLOCKS, CHUNK], fp32)
        h2 = sb("h2", [P, L2_BLOCKS, CHUNK], fp32)
        y = sb("y", [1, CHUNK], fp32)
        wp_high = sb("wp_high", [P, L1_BLOCKS, SLOTS, P], fp32r)
        wp_low = sb("wp_low", [P, L1_BLOCKS, SLOTS, P], fp32r)
        wd_high = sb("wd_high", [P, HIDDEN1], fp32r)
        wd_low = sb("wd_low", [P, HIDDEN1], fp32r)
        w2s = sb("w2s", [P, L1_BLOCKS, HIDDEN2], fp32)
        w3s = sb("w3s", [P, L2_BLOCKS], fp32)
        b1s = sb("b1s", [P, L1_BLOCKS], fp32)
        b2s = sb("b2s", [P, L2_BLOCKS], fp32)
        ident = sb("ident", [P, P], fp32)
        row_id = sb("row_id", [PICK_PARTS, PICK_PER_PART], fp32)
        tab_high = sb("tab_high", [PICK_PARTS, N, PICK_PER_PART, DIM], fp32r)
        tab_low = sb("tab_low", [PICK_PARTS, N, PICK_PER_PART, DIM], fp32r)
        ids32 = sb("ids32", [PICK_PARTS, N, CHUNK], i32)
        onehot = sb("onehot", [PICK_PARTS, ONEHOTS, PICK_PER_PART, CHUNK], fp32r)
        tab_raw = xt[0:PICK_PARTS, :, :, :].rearrange("p c s f -> p (c s f)").rearrange(
            "p (u n) -> p u n", n=PICK_PER_PART * DIM)
        wd_raw = h1[:].rearrange("p m s -> p (m s)")
        wp_raw = [wd_raw[:, 0:SLOTS * P], sb("wp_raw", [P, SLOTS * P], fp32)[:]]
        wd_sum = h2[:].rearrange("p m s -> p (m s)")

        p_tr = ctx.enter_context(nc.psum_tensor("p_tr", [P, 2, GROUP, P], fp32))
        p_gram = ctx.enter_context(nc.psum_tensor("p_gram", [P, 2, QUADS, P], fp32))
        p_out = ctx.enter_context(nc.psum_tensor("p_out", [P, 2, 512], fp32))

        idx_loaded = [sem(f"idx_loaded{c}") for c in range(2)]
        dense_loaded = [sem(f"dense_loaded{c}") for c in range(2)]
        rows_free = sem("rows_free")
        gathered = [[sem(f"gathered{c}_{g}") for g in range(NG)] for c in range(2)]
        ids_loaded = [sem(f"ids_loaded{h}") for h in range(2)]
        ident_loaded = sem("ident_loaded")
        row_id_loaded = sem("row_id_loaded")
        tab_loaded = [sem(f"tab_loaded{u}") for u in range(N)]
        weights_loaded = sem("weights_loaded")
        wp_loaded = [sem(f"wp_loaded{b}") for b in range(2)]
        wp_highs = sem("wp_highs")
        wp_lows = sem("wp_lows")
        wd_loaded = sem("wd_loaded")
        wd_added = sem("wd_added")
        wd_highs = sem("wd_highs")
        wd_lows = sem("wd_lows")
        zeroed = sem("zeroed")
        tab_highs = sem("tab_highs")
        tab_lows = sem("tab_lows")
        onehot_ready = sem("onehot_ready")
        transposed = [sem(f"transposed{b}") for b in range(2)]
        tr_taken = [sem(f"tr_taken{b}") for b in range(2)]
        gram_ready = sem("gram_ready")
        gram_taken = {"act": sem("gram_taken_act"), "dve": sem("gram_taken_dve")}
        highs_cut = sem("highs_cut")
        lows_cut = sem("lows_cut")
        out_ready = [sem(f"out_ready{b}") for b in range(2)]
        out_taken = [sem(f"out_taken{b}") for b in range(2)]
        y_stored = sem("y_stored")

        def wait(eng, s, count):
            if not isinstance(count, int) or count > 0:
                eng.wait_ge(s, count)

        def tr_count(i, c, g):
            return (2 * i + c) * HALF + g // 2

        def gram_count(i, c, k):
            return (TILES_PER_CHUNK * i + c) * GRAM_GROUPS + k

        PICK_USES = [(N + 1) // 2, N // 2]
        L1_USES = L1_BLOCKS // 2
        LAYER_USES = [L1_USES + 1 + 1, L1_USES + 1]

        def out_count(i, b, stage, n=0):
            before = {"pick": 0, "l1": PICK_USES[b], "l2": PICK_USES[b] + L1_USES,
                      "l3": PICK_USES[b] + L1_USES + 1}[stage]
            steps = 0 if isinstance(i, int) and i == 0 else i * PICK_USES[b] + (i - 1) * LAYER_USES[b]
            if isinstance(i, int) and i == CHUNKS and stage != "pick":
                before -= PICK_USES[b]
            return steps + before + n

        block = ctx.enter_context(nc.Block())

        @block.sync
        def _(sp):
            def load_tile(i, c):
                if not (isinstance(i, int) and i == 0):
                    wait(sp, transposed[0], tr_count(i - 1, c, NG))
                    wait(sp, transposed[1], tr_count(i - 1, c, NG))
                at = i * CHUNK + c * P
                sp.dma_start(idx[:, c, :], ids[bass.ds(at, P), :]).then_inc(idx_loaded[c], 16)
                sp.dma_start(rows[:, c, 0, :], dense[bass.ds(at, P), :]).then_inc(dense_loaded[c], 16)

            def load_ids(i, half):
                if not (isinstance(i, int) and i == 0):
                    wait(sp, onehot_ready, N * (i - 1) + (half + 1) * ONEHOTS)
                for u in range(half * ONEHOTS, (half + 1) * ONEHOTS):
                    sp.dma_start(ids32[:, u, :],
                                 ids_rows[PICKED[u]:PICKED[u] + 1, bass.ds(i * CHUNK, CHUNK)]
                                 .to_broadcast([PICK_PARTS, CHUNK])).then_inc(ids_loaded[half], 16)

            load_tile(0, 0)
            sp.dma_start(row_id[:], row_ids).then_inc(row_id_loaded, 16)
            for u in range(N):
                sp.dma_start(tab_raw[:, u, :], tables[PICKED[u]].rearrange("(p k) d -> p (k d)", k=PICK_PER_PART)
                             ).then_inc(tab_loaded[u], 16)
                if u == 0:
                    load_ids(0, 0)
            load_ids(0, 1)
            sp.dma_start(ident[:], identity).then_inc(ident_loaded, 16)
            load_tile(0, 1)
            with sp.Fori(1, CHUNKS) as i:
                load_ids(i, 0)
                load_tile(i, 0)
                load_ids(i, 1)
                load_tile(i, 1)

        @block.gpsimd
        def _(pool):
            def gather_tile(i, c):
                wait(pool, idx_loaded[c], 16 * (i + 1))
                for g, group in enumerate(GROUPS):
                    if not (isinstance(i, int) and i == 0):
                        wait(pool, transposed[g % 2], tr_count(i - 1, c, g) + 1)
                        pool.sem_inc(rows_free, 1)
                    for pos in group:
                        if pos:
                            f = GATHERED[pos - 1]
                            pool.indirect_dma_start(
                                rows[:, c, pos, :], None, tables[f],
                                bass.IndirectOffsetOnAxis(idx[:, c, f:f + 1], 0)).then_inc(gathered[c][g], 16)

            for c in range(TILES_PER_CHUNK):
                gather_tile(0, c)
            with pool.Fori(1, CHUNKS) as i:
                for c in range(TILES_PER_CHUNK):
                    gather_tile(i, c)

        @block.tensor
        def _(pe):
            def claim(i, b, stage, n=0):
                wait(pe, out_taken[b], out_count(i, b, stage, n))

            def pick(i, picks):
                for u in picks:
                    claim(i, u % 2, "pick", u // 2)
                    wait(pe, onehot_ready, N * i + u + 1)
                    if isinstance(i, int) and i == 0:
                        wait(pe, tab_lows, u + 1)
                    for k in range(PICK_PER_PART):
                        for part in (tab_high, tab_low):
                            last = nc.tensor.matmul(p_out[:, u % 2, 0:CHUNK], part[:, u, k, :],
                                                    onehot[:, u % ONEHOTS, k, :],
                                                    start=(k == 0 and part is tab_high),
                                                    stop=(k == PICK_PER_PART - 1 and part is tab_low))
                    last.then_inc(out_ready[u % 2], 1)

            def transpose(i, c, groups):
                for g in groups:
                    group = GROUPS[g]
                    if g == 0:
                        wait(pe, dense_loaded[c], 16 * (i + 1))
                    n_dma = len([pos for pos in group if pos])
                    wait(pe, gathered[c][g], 16 * n_dma * (i + 1))
                    wait(pe, tr_taken[g % 2], tr_count(i, c, g))
                    for q, pos in enumerate(group):
                        last = nc.tensor.transpose(p_tr[:, g % 2, q, :], rows[:, c, pos, :], ident[:])
                    last.then_inc(transposed[g % 2], 1)

            def gram_tile(i, c):
                if c == 0:
                    for b in range(2):
                        wait(pe, out_taken[b], out_count(i, b, "l1"))
                for b in range(2):
                    wait(pe, tr_taken[b], tr_count(i, c, NG))
                x = xt[:, c, :, :].rearrange("p (k q s) f -> p k q s f", s=BLOCKS, q=QUADS)
                for k in range(GRAM_GROUPS):
                    for taken in gram_taken.values():
                        wait(pe, taken, gram_count(i, c, k - 1))
                    for q in range(QUADS):
                        last = nc.tensor.matmul(p_gram[:, k % 2, q, 0:BLOCKS * SECONDS], x[:, k, q, :, :].rearrange("p s f -> p (s f)"),
                                                x[:, k, q, :, 1:1 + SECONDS], start=True, stop=True)
                    last.then_inc(gram_ready, 1)

            def layer1(i, m):
                if m == 0:
                    wait(pe, highs_cut, 2 * TILES_PER_CHUNK * i)
                claim(i, m % 2, "l1", m // 2)
                cols = slice(m * P, (m + 1) * P)
                terms = [(wd_high[:, cols], wd_low[:, cols], dense_high[:], dense_low[:])]
                terms += [(wp_high[:, m, k, :], wp_low[:, m, k, :], pairs_high[:, k, :], pairs_low[:, k, :])
                          for k in range(SLOTS)]
                for k, (w_high, w_low, x_high, x_low) in enumerate(terms):
                    nc.tensor.matmul(p_out[:, m % 2, 0:CHUNK], w_high, x_high, start=(k == 0), stop=False)
                    nc.tensor.matmul(p_out[:, m % 2, 0:CHUNK], w_low, x_high, start=False, stop=False)
                if m == 0:
                    wait(pe, lows_cut, 2 * TILES_PER_CHUNK * i)
                for k, (w_high, w_low, x_high, x_low) in enumerate(terms):
                    last = nc.tensor.matmul(p_out[:, m % 2, 0:CHUNK], w_high, x_low, start=False,
                                            stop=(k == SLOTS))
                last.then_inc(out_ready[m % 2], 1)

            def layer2(i, m):
                if m == 0:
                    for b in range(2):
                        wait(pe, out_taken[b], out_count(i, b, "l2"))
                for k in range(L1_BLOCKS):
                    last = nc.tensor.matmul(p_out[:, m, 0:CHUNK], w2s[:, k, m * P:(m + 1) * P], h1[:, k, :],
                                            start=(k == 0), stop=(k == L1_BLOCKS - 1))
                last.then_inc(out_ready[m], 1)

            def layer3(i):
                for b in range(2):
                    wait(pe, out_taken[b], out_count(i, b, "l3"))
                for k in range(L2_BLOCKS):
                    last = nc.tensor.matmul(p_out[0:1, 0, 0:CHUNK], w3s[:, k:k + 1], h2[:, k, :],
                                            start=(k == 0), stop=(k == L2_BLOCKS - 1))
                last.then_inc(out_ready[0], 1)

            thirds = [range(at, at + 2) for at in range(0, NG, 2)]

            def step(i, layers=True):
                pick(i, range(ONEHOTS))
                for n, groups in enumerate(thirds):
                    if isinstance(i, int) and n == 0:
                        wait(pe, ident_loaded, 16)
                    transpose(i, 0, groups)
                    pick(i, [ONEHOTS + n])
                if layers:
                    for m in range(L1_BLOCKS):
                        layer1(i, m)
                else:
                    wait(pe, zeroed, 2)
                gram_tile(i, 0)
                for m, groups in enumerate(thirds):
                    transpose(i, 1, groups)
                    if layers and m < L2_BLOCKS:
                        layer2(i, m)
                if layers:
                    layer3(i)
                gram_tile(i, 1)

            step(0, layers=False)
            wait(pe, weights_loaded, 4 * 16)
            wait(pe, wp_lows, L1_BLOCKS)
            wait(pe, wd_lows, 1)
            with pe.Fori(1, CHUNKS) as i:
                step(i)
            for m in range(L1_BLOCKS):
                layer1(CHUNKS, m)
            for m in range(L2_BLOCKS):
                layer2(CHUNKS, m)
            layer3(CHUNKS)

        def copy_group(copy, c, g, done):
            group = GROUPS[g]
            src = p_tr[:, g % 2, 0:len(group), :].rearrange("p f s -> p s f")
            copy(xt[:, c, :, group[0]:group[-1] + 1], src).then_inc(done, 1)

        def copy_gram(copy, c, k, blocks, done):
            x = pairs[:, :, c * P:(c + 1) * P].rearrange("p g (k q s) -> p g k s q", s=BLOCKS, q=QUADS)
            for s in blocks:
                for j in range(BLOCKS):
                    n = slots_of(j)
                    at = s * SECONDS + SLOTS * j
                    last = copy(x[32 * j:32 * j + 32, 0:n, k, s, :],
                                p_gram[32 * s:32 * s + 32, k % 2, :, at:at + n].rearrange("p q g -> p g q"))
            last.then_inc(done, 1)

        @block.scalar
        def _(act):
            copy = nc.scalar.copy

            def load_block(m):
                act.dma_start(wp_raw[m % 2], w_pairs[m]).then_inc(wp_loaded[m % 2], 16)

            for u in range(N):
                act.wait_ge(tab_loaded[u], 16)
                copy(tab_high[:, u, :, :].rearrange("p k d -> p (k d)"), tab_raw[:, u, :]).then_inc(tab_highs, 1)
            for m in range(2):
                load_block(m)
            for to, of in ((b1s, b1), (b2s, b2), (w3s, w3), (w2s, w2)):
                act.dma_start(to[:], of).then_inc(weights_loaded, 16)

            def cut_block(m):
                act.wait_ge(wp_loaded[m % 2], 16 * (m // 2 + 1))
                copy(wp_high[:, m, :, :].rearrange("p k n -> p (k n)"), wp_raw[m % 2]).then_inc(wp_highs, 1)

            def cut_weights():
                for m in range(2):
                    act.wait_ge(wp_lows, m + 1)
                    load_block(m + 2)
                for m in range(2, L1_BLOCKS):
                    cut_block(m)
                act.wait_ge(wp_lows, 3)
                act.dma_start(wd_raw, w_dense).then_inc(wd_loaded, 16)
                act.wait_ge(wd_added, 1)
                copy(wd_high[:], wd_sum).then_inc(wd_highs, 1)

            def take_picked(i, picks):
                for u in picks:
                    b = u % 2
                    act.wait_ge(out_ready[b], out_count(i, b, "pick", u // 2 + 1))
                    copy(xt[:, :, :, MOVED + u],
                         p_out[:, b, 0:CHUNK].rearrange("p (c s) -> p c s", c=2)).then_inc(out_taken[b], 1)

            def take_transposes(i, c, groups):
                for g in groups:
                    act.wait_ge(transposed[1], tr_count(i, c, g) + 1)
                    copy_group(copy, c, g, tr_taken[1])

            def take_gram(i, c):
                if c == 0:
                    wait(act, lows_cut, 2 * TILES_PER_CHUNK * i)
                for k in range(GRAM_GROUPS):
                    act.wait_ge(gram_ready, gram_count(i, c, k + 1))
                    copy_gram(copy, c, k, (0, 1), gram_taken["act"])

            def cut_highs(i, c):
                at = slice(c * P, (c + 1) * P)
                act.wait_ge(tr_taken[0], tr_count(i, c, 0) + 1)
                copy(dense_high[:, at], xt[:, c, :, 0]).then_inc(highs_cut, 1)
                for taken in gram_taken.values():
                    act.wait_ge(taken, gram_count(i, c, GRAM_GROUPS))
                copy(pairs_high[:, :, at], pairs[:, :, at]).then_inc(highs_cut, 1)

            def take_layer1(i, blocks=range(L1_BLOCKS)):
                for m in blocks:
                    act.wait_ge(out_ready[m % 2], out_count(i, m % 2, "l1", m // 2 + 1))
                    nc.scalar.activation(h1[:, m, :], p_out[:, m % 2, 0:CHUNK], ACT.Relu,
                                         bias=b1s[:, m:m + 1]).then_inc(out_taken[m % 2], 1)

            def take_layer2(i, blocks=range(L2_BLOCKS)):
                for m in blocks:
                    act.wait_ge(out_ready[m], out_count(i, m, "l2", 1))
                    nc.scalar.activation(h2[:, m, :], p_out[:, m, 0:CHUNK], ACT.Relu,
                                         bias=b2s[:, m:m + 1]).then_inc(out_taken[m], 1)

            def take_layer3(i):
                act.wait_ge(out_ready[0], out_count(i, 0, "l3", 1))
                if not (isinstance(i, int) and i == 1):
                    act.wait_ge(y_stored, 16 * (i - 1))
                copy(y[:], p_out[0:1, 0, 0:CHUNK]).then_inc(out_taken[0], 1)
                act.wait_ge(out_taken[0], out_count(i, 0, "l3", 1))
                act.dma_start(out[:, bass.ds((i - 1) * CHUNK, CHUNK)], y[:]).then_inc(y_stored, 16)

            def step(i, layers=True):
                take_picked(i, range(ONEHOTS))
                for n in range(HALF):
                    take_transposes(i, 0, [2 * n + 1])
                    take_picked(i, [ONEHOTS + n])
                if layers:
                    take_layer1(i)
                take_gram(i, 0)
                cut_highs(i, 0)
                if not layers:
                    cut_weights()
                for n in range(HALF):
                    take_transposes(i, 1, [2 * n + 1])
                    if layers and n < L2_BLOCKS:
                        take_layer2(i, [n])
                if layers:
                    take_layer3(i)
                take_gram(i, 1)
                cut_highs(i, 1)

            act.wait_ge(tab_lows, N)
            for m in range(2):
                cut_block(m)
            step(0, layers=False)
            act.wait_ge(weights_loaded, 4 * 16)
            with act.Fori(1, CHUNKS) as i:
                step(i)
            take_layer1(CHUNKS)
            take_layer2(CHUNKS)
            take_layer3(CHUNKS)
            act.wait_ge(y_stored, 16 * CHUNKS)

        @block.vector
        def _(dve):
            copy = nc.vector.tensor_copy

            def make_onehots(i, half, tables):
                dve.wait_ge(ids_loaded[half], 16 * ONEHOTS * (i + 1))
                for u in tables:
                    if not (isinstance(i, int) and i == 0 and half == 0):
                        step_before, before = (i, u - ONEHOTS) if half else (i - 1, u + ONEHOTS)
                        dve.wait_ge(out_ready[before % 2], out_count(step_before, before % 2, "pick", before // 2 + 1))
                    for k in range(PICK_PER_PART):
                        last = nc.vector.tensor_scalar(onehot[:, u % ONEHOTS, k, :], ids32[:, u, :],
                                                       row_id[:, k:k + 1], None, ALU.is_equal)
                    last.then_inc(onehot_ready, 1)

            def cut_lows(i, c):
                at = slice(c * P, (c + 1) * P)
                dve.wait_ge(highs_cut, 2 * (TILES_PER_CHUNK * i + c) + 1)
                nc.vector.tensor_tensor(dense_low[:, at], xt[:, c, :, 0], dense_high[:, at].bitcast(fp32),
                                        ALU.subtract).then_inc(lows_cut, 1)
                dve.wait_ge(highs_cut, 2 * (TILES_PER_CHUNK * i + c) + 2)
                nc.vector.tensor_tensor(pairs_low[:, :, at], pairs[:, :, at], pairs_high[:, :, at].bitcast(fp32),
                                        ALU.subtract).then_inc(lows_cut, 1)

            def take_transposes(i, c, groups=range(0, NG, 2)):
                for g in groups:
                    dve.wait_ge(transposed[0], tr_count(i, c, g) + 1)
                    copy_group(copy, c, g, tr_taken[0])

            def take_gram(i, c):
                if c == 0 and not (isinstance(i, int) and i == 0):
                    dve.wait_ge(out_ready[1], out_count(i, 1, "l1", L1_USES))
                    wait(dve, highs_cut, 2 * TILES_PER_CHUNK * i)
                for k in range(GRAM_GROUPS):
                    dve.wait_ge(gram_ready, gram_count(i, c, k + 1))
                    copy_gram(copy, c, k, (2, 3), gram_taken["dve"])

            later = range(ONEHOTS, N)

            def step(i, first=False, last=False):
                make_onehots(i, 1, later[:1])
                if not first:
                    cut_lows(i - 1, 1)
                for n in range(HALF):
                    take_transposes(i, 0, [2 * n])
                    if n + 1 < len(later):
                        make_onehots(i, 1, [later[n + 1]])
                if not last:
                    make_onehots(i + 1, 0, range(ONEHOTS))
                take_gram(i, 0)
                cut_lows(i, 0)
                if first:
                    cut_weights()
                take_transposes(i, 1)
                take_gram(i, 1)

            def cut_table(u):
                dve.wait_ge(tab_highs, u + 1)
                nc.vector.tensor_tensor(tab_low[:, u, :, :].rearrange("p k d -> p (k d)"), tab_raw[:, u, :],
                                        tab_high[:, u, :, :].rearrange("p k d -> p (k d)").bitcast(fp32),
                                        ALU.subtract).then_inc(tab_lows, 1)

            def cut_block(m):
                dve.wait_ge(wp_highs, m + 1)
                nc.vector.tensor_tensor(wp_low[:, m, :, :].rearrange("p k n -> p (k n)"), wp_raw[m % 2],
                                        wp_high[:, m, :, :].rearrange("p k n -> p (k n)").bitcast(fp32),
                                        ALU.subtract).then_inc(wp_lows, 1)

            def cut_weights():
                for m in range(2, L1_BLOCKS):
                    cut_block(m)
                dve.wait_ge(wd_loaded, 16)
                nc.vector.tensor_tensor(wd_sum, wd_raw[:, 0:HIDDEN1], wd_raw[:, HIDDEN1:], ALU.add
                                        ).then_inc(wd_added, 1)
                dve.wait_ge(wd_highs, 1)
                nc.vector.tensor_tensor(wd_low[:], wd_sum, wd_high[:].bitcast(fp32), ALU.subtract
                                        ).then_inc(wd_lows, 1)

            nc.vector.memset(pairs[:, slots_of(BLOCKS - 1):, :], 0.0).then_inc(zeroed, 1)
            for u in range(2):
                cut_table(u)
            dve.wait_ge(row_id_loaded, 16)
            make_onehots(0, 0, [0])
            for u in range(2, N):
                cut_table(u)
            make_onehots(0, 0, range(1, ONEHOTS))
            dve.wait_ge(tab_lows, N)
            nc.vector.memset(xt[:, :, :, FEATURES:], 0.0).then_inc(zeroed, 1)
            for m in range(2):
                cut_block(m)
            step(0, first=True)
            with dve.Fori(1, CHUNKS - 1) as i:
                step(i)
            step(CHUNKS - 1, last=True)
            cut_lows(CHUNKS - 1, 1)


def kernel(**inputs):
    import numpy as np
    import concourse.bacc as bacc
    from concourse import mybir as _mybir
    from concourse.bass_utils import run_bass_kernel_spmd

    nc = bacc.Bacc("TRN2", target_bir_lowering=False, num_devices=1)
    arrays = {}

    def give(name, a):
        a = np.ascontiguousarray(a)
        arrays[name] = a
        return nc.dram_tensor(name, a.shape, _mybir.dt.from_np(a.dtype), kind="ExternalInput").ap()

    ids = np.asarray(inputs["ids"])
    w1 = np.asarray(inputs["W_top1"])
    n_pairs = FEATURES * (FEATURES - 1) // 2
    w_pairs = np.zeros((BLOCKS, 32, SLOTS, HIDDEN1), w1.dtype)
    for b in range(1, FEATURES):
        j, slot = (b - 1) // SLOTS, (b - 1) % SLOTS
        for a in range(b):
            f, g = sorted((ORDER[a], ORDER[b]))
            w_pairs[j, a, slot] = w1[DIM + f * FEATURES - f * (f + 1) // 2 + g - f - 1]
    w_dense = np.stack([w1[:DIM], w1[DIM + n_pairs:]], axis=1)
    out = nc.dram_tensor("y_out", (BATCH, 1), _mybir.dt.from_np(w1.dtype), kind="ExternalOutput").ap()
    build(
        nc,
        dense=give("dense", inputs["r_dense_features"]),
        ids=give("ids", ids),
        ids_rows=give("ids_rows", ids.T),
        tables=[give(f"tbl_{f}", inputs[f"tbl_{f}"]) for f in range(NUM_TABLES)],
        w_pairs=give("w_pairs", w_pairs.reshape(P, SLOTS, L1_BLOCKS, P).transpose(2, 0, 1, 3).reshape(
            L1_BLOCKS, P, SLOTS * P)),
        w_dense=give("w_dense", w_dense.reshape(P, 2 * HIDDEN1)),
        b1=give("b1", np.asarray(inputs["b_top1"]).reshape(L1_BLOCKS, P).T),
        w2=give("w2", np.asarray(inputs["W_top2"]).reshape(L1_BLOCKS, P, HIDDEN2).transpose(1, 0, 2)),
        b2=give("b2", np.asarray(inputs["b_top2"]).reshape(L2_BLOCKS, P).T),
        w3=give("w3", np.asarray(inputs["W_top3"]).reshape(L2_BLOCKS, P).T),
        identity=give("identity", np.eye(P, dtype=np.float32)),
        row_ids=give("row_ids", np.arange(PICK_ROWS, dtype=np.float32).reshape(PICK_PARTS, PICK_PER_PART)),
        out=out.rearrange("b o -> o b"),
    )
    r = run_bass_kernel_spmd(nc, [arrays], core_ids=[0])
    return r.results[0]["y_out"]
```

```python
import concourse.bass as bass
from concourse import mybir
from contextlib import ExitStack

NUM_TABLES = 26
FEATURES = NUM_TABLES + 1
DIM = 128
P = 128
BATCH = 2048
CHUNK = 256
CHUNKS = BATCH // CHUNK
TILES_PER_CHUNK = CHUNK // P
HIDDEN1, HIDDEN2 = 512, 256
ROWS = [125000, 1000, 12500, 1250, 1000, 1000, 12500, 1250, 1000, 1250, 1000, 12500, 12500, 12500,
        1000, 1000, 12500, 1000, 12500, 1000, 1000, 1250, 1250, 1250, 12500, 1250]

PICKED = [1, 4, 5, 8, 10, 14]
assert all(ROWS[f] == 1000 for f in PICKED)
GATHERED = [f for f in range(NUM_TABLES) if f not in PICKED]
PICK_ROWS = 1000
PICK_PARTS = 125
PICK_PER_PART = PICK_ROWS // PICK_PARTS
ONEHOTS = 3
HALVES = [range(ONEHOTS), range(ONEHOTS, len(PICKED))]
PICKED_AHEAD = [0, 1]
PICKED_AFTER = [[2, 3], [4], [5]]

ORDER = [0] + [1 + f for f in GATHERED] + [1 + f for f in PICKED]
MOVED = 1 + len(GATHERED)
POSITIONS = 32
DENSE_AGAIN = FEATURES
GROUP = 4
GROUPS = [[0, 1, 2, 3], [4, 5, 6, 7], [8, 9, 10, 11], [12, 13, 14, 15], [16, 17, 18, 19], [20]]
assert sum(GROUPS, []) == list(range(MOVED)) and max(map(len, GROUPS)) <= GROUP
BLOCKS = 4
SLOTS = 7
SECONDS = FEATURES - 1
QUADS = 8
GRAM_GROUPS = P // (BLOCKS * QUADS)
L1_BLOCKS, L2_BLOCKS = HIDDEN1 // P, HIDDEN2 // P


def slots_of(j):
    return min(SLOTS, SECONDS - SLOTS * j)


def build(nc, dense, ids, ids_rows, tables, w_pairs, w_dense, b1, w2, b2, w3, identity, row_ids, sides, out):
    fp32, fp32r, i32 = mybir.dt.float32, mybir.dt.float32r, mybir.dt.int32
    ALU = mybir.AluOpType
    ACT = mybir.ActivationFunctionType
    N = len(PICKED)
    NG = len(GROUPS)
    assert NG % 2 == 0, "each bank of transposes serves every second group"
    HALF = NG // 2

    ctx = ExitStack()
    with ctx:
        def sb(name, shape, dt):
            return ctx.enter_context(nc.sbuf_tensor(name, shape, dt))

        def sem(name):
            return ctx.enter_context(nc.semaphore(name))

        idx = sb("idx", [P, 2, 2, NUM_TABLES], i32)
        rows = sb("rows", [P, 2, MOVED, DIM], fp32)
        xt = sb("xt", [P, 2, P, POSITIONS], fp32)
        pairs = sb("pairs", [P, SLOTS, P], fp32)
        pairs_high = sb("pairs_high", [P, SLOTS, CHUNK], fp32r)
        pairs_low = sb("pairs_low", [P, SLOTS, CHUNK], fp32r)
        dense_high = sb("dense_high", [P, CHUNK], fp32r)
        dense_low = sb("dense_low", [P, CHUNK], fp32r)
        hidden = sb("hidden", [P, 4, CHUNK], fp32)
        h1, h2 = hidden[:, 0:2, :], hidden[:, 2:4, :]
        h1_high = sb("h1_high", [P, L1_BLOCKS, CHUNK], fp32r)
        h1_low = sb("h1_low", [P, L1_BLOCKS, CHUNK], fp32r)
        wp = sb("wp", [P, SLOTS, HIDDEN1], fp32r)
        wd_high = sb("wd_high", [P, HIDDEN1], fp32r)
        wd_low = sb("wd_low", [P, HIDDEN1], fp32r)
        w2_high = sb("w2_high", [P, L1_BLOCKS, HIDDEN2], fp32r)
        w2_low = sb("w2_low", [P, L1_BLOCKS, HIDDEN2], fp32r)
        w3s = sb("w3s", [P, L2_BLOCKS], fp32)
        side = sb("side", [P, 2, SLOTS], fp32)
        b1s = sb("b1s", [P, L1_BLOCKS], fp32)
        b2s = sb("b2s", [P, L2_BLOCKS], fp32)
        ident = sb("ident", [P, P], fp32)
        row_id = sb("row_id", [PICK_PARTS, PICK_PER_PART], fp32)
        tab_high = sb("tab_high", [PICK_PARTS, N, PICK_PER_PART, DIM], fp32r)
        tab_low = sb("tab_low", [PICK_PARTS, N, PICK_PER_PART, DIM], fp32r)
        ids32 = sb("ids32", [PICK_PARTS, N, CHUNK], i32)
        onehot = sb("onehot", [PICK_PARTS, ONEHOTS, PICK_PER_PART, CHUNK], fp32r)
        tab_raw = xt[0:PICK_PARTS, :, :, :].rearrange("p c s f -> p (c s f)").rearrange(
            "p (u n) -> p u n", n=PICK_PER_PART * DIM)
        w_raw = sb("w_raw", [P, L1_BLOCKS * HIDDEN2], fp32)
        y = w_raw[0:1, 0:CHUNK]
        raw = {"pairs": pairs[:].rearrange("p k s -> p (k s)"), "hidden": hidden[:].rearrange("p m s -> p (m s)"),
               "w_raw": w_raw[:]}
        PAIR_CUTS = [("pairs", 6, 1), ("hidden", 0, 2), ("w_raw", 2, 2), ("hidden", 4, 2)]
        CUTS = [(held, w_pairs[:, at:at + n, :].rearrange("p k n -> p (k n)"), n * HIDDEN1, None, None)
                for held, at, n in PAIR_CUTS]
        CUTS += [("w_raw", w_dense, 2 * HIDDEN1, wd_high[:], wd_low[:]),
                 ("hidden", w2, L1_BLOCKS * HIDDEN2, w2_high[:].rearrange("p k n -> p (k n)"),
                  w2_low[:].rearrange("p k n -> p (k n)"))]
        DENSE_CUT = len(PAIR_CUTS)
        wd_sum = raw["w_raw"][:, 0:HIDDEN1]

        p_tr = ctx.enter_context(nc.psum_tensor("p_tr", [P, 2, GROUP, P], fp32))
        p_gram = ctx.enter_context(nc.psum_tensor("p_gram", [P, 2, QUADS, P], fp32))
        p_out = ctx.enter_context(nc.psum_tensor("p_out", [P, 2, 512], fp32))

        idx_loaded = [[sem(f"idx_loaded{e}_{c}") for c in range(2)] for e in range(2)]
        dense_loaded = [sem(f"dense_loaded{c}") for c in range(2)]
        rows_free = sem("rows_free")
        gathered = [[sem(f"gathered{c}_{g}") for g in range(NG)] for c in range(2)]
        ids_loaded = [sem(f"ids_loaded{h}") for h in range(2)]
        ident_loaded = sem("ident_loaded")
        row_id_loaded = sem("row_id_loaded")
        tab_loaded = [sem(f"tab_loaded{u}") for u in range(N)]
        weights_loaded = sem("weights_loaded")
        raw_loaded = [sem(f"raw_loaded{n}") for n in range(len(CUTS))]
        side_loaded = sem("side_loaded")
        w_highs = sem("w_highs")
        w_lows = sem("w_lows")
        wd_added = sem("wd_added")
        zeroed = sem("zeroed")
        tab_highs = sem("tab_highs")
        tab_lows = sem("tab_lows")
        onehot_ready = sem("onehot_ready")
        transposed = [sem(f"transposed{b}") for b in range(2)]
        tr_taken = [sem(f"tr_taken{b}") for b in range(2)]
        gram_ready = sem("gram_ready")
        gram_taken = {"act": sem("gram_taken_act"), "dve": sem("gram_taken_dve")}
        highs_cut = sem("highs_cut")
        lows_cut = sem("lows_cut")
        h1_highs = sem("h1_highs")
        h1_lows = sem("h1_lows")
        out_ready = [sem(f"out_ready{b}") for b in range(2)]
        out_taken = [sem(f"out_taken{b}") for b in range(2)]
        y_stored = sem("y_stored")

        def pair_cut(n):
            held, at, slots = PAIR_CUTS[n]
            return [(at + k, raw[held][:, k * HIDDEN1:(k + 1) * HIDDEN1]) for k in range(slots)]

        def wait(eng, s, count):
            if not isinstance(count, int) or count > 0:
                eng.wait_ge(s, count)

        def tr_count(i, c, g):
            return (2 * i + c) * HALF + g // 2

        def gram_count(i, c, k):
            return (TILES_PER_CHUNK * i + c) * GRAM_GROUPS + k

        PICK_USES = [(N + 1) // 2, N // 2]
        L1_USES = L1_BLOCKS // 2
        LAYER_USES = [L1_USES + 1, L1_USES + 1 + 1]

        def out_count(i, b, stage, n=0):
            before = {"pick": 0, "l1": PICK_USES[b], "l2": PICK_USES[b] + L1_USES,
                      "l3": PICK_USES[b] + L1_USES + 1}[stage]
            steps = 0 if isinstance(i, int) and i == 0 else i * PICK_USES[b] + (i - 1) * LAYER_USES[b]
            if isinstance(i, int) and i == CHUNKS and stage != "pick":
                before -= PICK_USES[b]
            return steps + before + n

        block = ctx.enter_context(nc.Block())

        @block.sync
        def _(sp):
            def load_indices(j, e, c):
                if not (isinstance(j, int) and j == 0):
                    wait(sp, transposed[0], tr_count(2 * (j - 1) + e, c, NG))
                    wait(sp, transposed[1], tr_count(2 * (j - 1) + e, c, NG))
                sp.dma_start(idx[:, e, c, :], ids[bass.ds((2 * j + e) * CHUNK + c * P, P), :]
                             ).then_inc(idx_loaded[e][c], 16)

            def load_dense(i, c):
                if not (isinstance(i, int) and i == 0):
                    wait(sp, transposed[0], tr_count(i - 1, c, 0) + 1)
                sp.dma_start(rows[:, c, 0, :], dense[bass.ds(i * CHUNK + c * P, P), :]).then_inc(dense_loaded[c], 16)

            def load_tile(j, e, c):
                load_indices(j, e, c)
                load_dense(2 * j + e, c)

            def load_ids(i, half):
                if not (isinstance(i, int) and i == 0):
                    wait(sp, onehot_ready, N * (i - 1) + HALVES[half][-1] + 1)
                for u in HALVES[half]:
                    sp.dma_start(ids32[:, u, :],
                                 ids_rows[PICKED[u]:PICKED[u] + 1, bass.ds(i * CHUNK, CHUNK)]
                                 .to_broadcast([PICK_PARTS, CHUNK])).then_inc(ids_loaded[half], 16)

            load_indices(0, 0, 0)
            for u in range(N):
                sp.dma_start(tab_raw[:, u, :], tables[PICKED[u]].rearrange("(p k) d -> p (k d)", k=PICK_PER_PART)
                             ).then_inc(tab_loaded[u], 16)
                if u == 0:
                    sp.dma_start(row_id[:], row_ids).then_inc(row_id_loaded, 16)
                    load_ids(0, 0)
            load_ids(0, 1)
            load_dense(0, 0)
            sp.dma_start(ident[:], identity).then_inc(ident_loaded, 16)
            load_tile(0, 0, 1)

            def load_chunk(j, e):
                for c in range(TILES_PER_CHUNK):
                    load_ids(2 * j + e, c)
                    load_tile(j, e, c)

            load_chunk(0, 1)
            with sp.Fori(1, CHUNKS // 2) as j:
                for e in range(2):
                    load_chunk(j, e)

        @block.gpsimd
        def _(pool):
            def gather_tile(j, e, c):
                i = 2 * j + e
                wait(pool, idx_loaded[e][c], 16 * (j + 1))
                for g, group in enumerate(GROUPS):
                    if not (isinstance(i, int) and i == 0):
                        wait(pool, transposed[g % 2], tr_count(i - 1, c, g) + 1)
                        pool.sem_inc(rows_free, 1)
                    for pos in group:
                        if pos:
                            f = GATHERED[pos - 1]
                            pool.indirect_dma_start(
                                rows[:, c, pos, :], None, tables[f],
                                bass.IndirectOffsetOnAxis(idx[:, e, c, f:f + 1], 0)).then_inc(gathered[c][g], 16)

            def gather_chunk(j, e):
                for c in range(TILES_PER_CHUNK):
                    gather_tile(j, e, c)

            for e in range(2):
                gather_chunk(0, e)
            with pool.Fori(1, CHUNKS // 2) as j:
                for e in range(2):
                    gather_chunk(j, e)

        @block.tensor
        def _(pe):
            def claim(i, b, stage, n=0):
                wait(pe, out_taken[b], out_count(i, b, stage, n))

            def pick(i, picks):
                for u in picks:
                    claim(i, u % 2, "pick", u // 2)
                    wait(pe, onehot_ready, N * i + u + 1)
                    if isinstance(i, int) and i == 0:
                        wait(pe, tab_lows, u + 1)
                    for k in range(PICK_PER_PART):
                        for part in (tab_high, tab_low):
                            last = nc.tensor.matmul(p_out[:, u % 2, 0:CHUNK], part[:, u, k, :],
                                                    onehot[:, u % ONEHOTS, k, :],
                                                    start=(k == 0 and part is tab_high),
                                                    stop=(k == PICK_PER_PART - 1 and part is tab_low))
                    last.then_inc(out_ready[u % 2], 1)

            def transpose(i, c, groups):
                for g in groups:
                    group = GROUPS[g]
                    if g == 0:
                        wait(pe, dense_loaded[c], 16 * (i + 1))
                    n_dma = len([pos for pos in group if pos])
                    wait(pe, gathered[c][g], 16 * n_dma * (i + 1))
                    wait(pe, tr_taken[g % 2], tr_count(i, c, g))
                    for q, pos in enumerate(group):
                        last = nc.tensor.transpose(p_tr[:, g % 2, q, :], rows[:, c, pos, :], ident[:])
                    last.then_inc(transposed[g % 2], 1)

            def gram_tile(i, c):
                if c == 0:
                    for b in range(2):
                        wait(pe, out_taken[b], out_count(i, b, "l1"))
                for b in range(2):
                    wait(pe, tr_taken[b], tr_count(i, c, NG))
                x = xt[:, c, :, :].rearrange("p (k q s) f -> p k q s f", s=BLOCKS, q=QUADS)
                for k in range(GRAM_GROUPS):
                    for taken in gram_taken.values():
                        wait(pe, taken, gram_count(i, c, k - 1))
                    for q in range(QUADS):
                        last = nc.tensor.matmul(p_gram[:, k % 2, q, 0:BLOCKS * SECONDS],
                                                x[:, k, q, :, :].rearrange("p s f -> p (s f)"),
                                                x[:, k, q, :, 1:1 + SECONDS], start=True, stop=True)
                    last.then_inc(gram_ready, 1)

            def layer1(i, m):
                if m == 0:
                    wait(pe, w_lows, DENSE_CUT + 1)
                    wait(pe, highs_cut, 3 * TILES_PER_CHUNK * i - 2)
                claim(i, m % 2, "l1", m // 2)
                cols = slice(m * P, (m + 1) * P)
                out = p_out[:, m % 2, 0:CHUNK]
                nc.tensor.matmul(out, wd_high[:, cols], dense_high[:], start=True, stop=False)
                nc.tensor.matmul(out, wd_low[:, cols], dense_high[:], start=False, stop=False)
                if m == 0:
                    wait(pe, highs_cut, 3 * TILES_PER_CHUNK * i)
                for k in range(SLOTS):
                    nc.tensor.matmul(out, wp[:, k, cols], pairs_high[:, k, :], start=False, stop=False)
                if m == 0:
                    wait(pe, lows_cut, 2 * TILES_PER_CHUNK * i)
                nc.tensor.matmul(out, wd_high[:, cols], dense_low[:], start=False, stop=False)
                for k in range(SLOTS):
                    last = nc.tensor.matmul(out, wp[:, k, cols], pairs_low[:, k, :], start=False,
                                            stop=(k == SLOTS - 1))
                last.then_inc(out_ready[m % 2], 1)

            def layer2(i, m, blocks=range(L1_BLOCKS)):
                if 0 in blocks:
                    if m == 0:
                        wait(pe, w_lows, len(CUTS))
                    wait(pe, out_taken[m], out_count(i, m, "l2"))
                cols = slice(m * P, (m + 1) * P)
                out = p_out[:, m, 0:CHUNK]
                for k in blocks:
                    if m == 0:
                        wait(pe, h1_highs, L1_BLOCKS * (i - 1) + k + 1)
                    nc.tensor.matmul(out, w2_high[:, k, cols], h1_high[:, k, :], start=(k == 0), stop=False)
                    nc.tensor.matmul(out, w2_low[:, k, cols], h1_high[:, k, :], start=False, stop=False)
                for k in blocks:
                    if m == 0:
                        wait(pe, h1_lows, L1_BLOCKS * (i - 1) + k + 1)
                    last = nc.tensor.matmul(out, w2_high[:, k, cols], h1_low[:, k, :], start=False,
                                            stop=(k == L1_BLOCKS - 1))
                if L1_BLOCKS - 1 in blocks:
                    last.then_inc(out_ready[m], 1)

            def layer3(i):
                for b in range(2):
                    wait(pe, out_taken[b], out_count(i, b, "l3"))
                for k in range(L2_BLOCKS):
                    last = nc.tensor.matmul(p_out[0:1, 1, 0:CHUNK], w3s[:, k:k + 1], h2[:, k, :],
                                            start=(k == 0), stop=(k == L2_BLOCKS - 1))
                last.then_inc(out_ready[1], 1)

            thirds = [range(at, at + 2) for at in range(0, NG, 2)]

            def step(i, layers=True, last=False):
                for n, groups in enumerate(thirds):
                    if isinstance(i, int) and i == 0 and n == 0:
                        wait(pe, ident_loaded, 16)
                    transpose(i, 0, groups)
                    pick(i, PICKED_AFTER[n])
                if layers:
                    for m in range(L1_BLOCKS):
                        layer1(i, m)
                else:
                    wait(pe, zeroed, 2)
                gram_tile(i, 0)
                if not layers:
                    pick(i + 1, PICKED_AHEAD)
                for m, groups in enumerate(thirds):
                    transpose(i, 1, groups)
                    if layers and m < L2_BLOCKS:
                        layer2(i, m)
                if layers:
                    layer3(i)
                    if not last:
                        pick(i + 1, PICKED_AHEAD)
                gram_tile(i, 1)

            pick(0, PICKED_AHEAD)
            step(0, layers=False)
            wait(pe, weights_loaded, 3 * 16)
            with pe.Fori(1, CHUNKS - 1) as i:
                step(i)
            step(CHUNKS - 1, last=True)
            for m in range(L1_BLOCKS):
                layer1(CHUNKS, m)
            for blocks in (range(L1_BLOCKS - 1), [L1_BLOCKS - 1]):
                for m in range(L2_BLOCKS):
                    layer2(CHUNKS, m, blocks)
            layer3(CHUNKS)

        def copy_group(copy, c, g, done):
            group = GROUPS[g]
            src = p_tr[:, g % 2, 0:len(group), :].rearrange("p f s -> p s f")
            if g == 0:
                copy(xt[:, c, :, DENSE_AGAIN], p_tr[:, 0, 0, :])
            copy(xt[:, c, :, group[0]:group[-1] + 1], src).then_inc(done, 1)

        def copy_gram(copy, k, blocks, done):
            x = pairs[:].rearrange("p g (k q s) -> p g k s q", s=BLOCKS, q=QUADS)
            for s in blocks:
                for j in range(BLOCKS):
                    n = slots_of(j)
                    at = s * SECONDS + SLOTS * j
                    last = copy(x[32 * j:32 * j + 32, 0:n, k, s, :],
                                p_gram[32 * s:32 * s + 32, k % 2, :, at:at + n].rearrange("p q g -> p g q"))
            last.then_inc(done, 1)

        @block.scalar
        def _(act):
            copy = nc.scalar.copy

            def load_raw(n):
                held, dram, width, _, _ = CUTS[n]
                before = [m for m in range(n) if CUTS[m][0] == held]
                if before:
                    act.wait_ge(w_lows, before[-1] + 1)
                act.dma_start(raw[held][:, 0:width], dram).then_inc(raw_loaded[n], 16)

            act.dma_start(side[:], sides).then_inc(side_loaded, 16)
            for u in range(N):
                act.wait_ge(tab_loaded[u], 16)
                copy(tab_high[:, u, :, :].rearrange("p k d -> p (k d)"), tab_raw[:, u, :]).then_inc(tab_highs, 1)
            for n in range(3):
                load_raw(n)
            for to, of in ((b1s, b1), (b2s, b2), (w3s, w3)):
                act.dma_start(to[:], of).then_inc(weights_loaded, 16)

            def cut_weights(cuts):
                for n in cuts:
                    held, _, width, high, _ = CUTS[n]
                    if n == DENSE_CUT:
                        act.wait_ge(wd_added, 1)
                        copy(high, wd_sum).then_inc(w_highs, 1)
                        continue
                    act.wait_ge(raw_loaded[n], 16)
                    if n < len(PAIR_CUTS):
                        for k, w in pair_cut(n):
                            last = nc.scalar.mul(wp[:, k, :], w, side[:, 0, k:k + 1])
                        last.then_inc(w_highs, 1)
                    else:
                        copy(high, raw[held][:, 0:width]).then_inc(w_highs, 1)

            def take_picked(i, picks):
                for u in picks:
                    b = u % 2
                    act.wait_ge(out_ready[b], out_count(i, b, "pick", u // 2 + 1))
                    copy(xt[:, :, :, MOVED + u],
                         p_out[:, b, 0:CHUNK].rearrange("p (c s) -> p c s", c=2)).then_inc(out_taken[b], 1)

            def take_transposes(i, c, groups):
                for g in groups:
                    act.wait_ge(transposed[g % 2], tr_count(i, c, g) + 1)
                    copy_group(copy, c, g, tr_taken[g % 2])

            def take_gram(i, c):
                act.wait_ge(tr_taken[0], tr_count(i, c, 0) + 1)
                copy(dense_high[:, c * P:(c + 1) * P], xt[:, c, :, 0]).then_inc(highs_cut, 1)
                wait(act, lows_cut, 2 * (TILES_PER_CHUNK * i + c))
                most = P // GRAM_GROUPS * (GRAM_GROUPS - 1)
                for k in range(GRAM_GROUPS):
                    act.wait_ge(gram_ready, gram_count(i, c, k + 1))
                    copy_gram(copy, k, (0, 1), gram_taken["act"])
                    if isinstance(i, int) and i == 0 and c == 0:
                        copy_gram(copy, k, (2, 3), gram_taken["dve"])
                    if k >= GRAM_GROUPS - 2:
                        for taken in gram_taken.values():
                            act.wait_ge(taken, gram_count(i, c, k + 1))
                        at, to = (0, most) if k < GRAM_GROUPS - 1 else (most, P)
                        copy(pairs_high[:, :, c * P + at:c * P + to], pairs[:, :, at:to]).then_inc(highs_cut, 1)

            def take_layer1(i):
                for m in range(L1_BLOCKS):
                    act.wait_ge(out_ready[m % 2], out_count(i, m % 2, "l1", m // 2 + 1))
                    if m >= 2:
                        act.wait_ge(h1_lows, L1_BLOCKS * (i - 1) + m - 1)
                    nc.scalar.activation(h1[:, m % 2, :], p_out[:, m % 2, 0:CHUNK], ACT.Relu,
                                         bias=b1s[:, m:m + 1]).then_inc(out_taken[m % 2], 1)
                    act.wait_ge(out_taken[m % 2], out_count(i, m % 2, "l1", m // 2 + 1))
                    copy(h1_high[:, m, :], h1[:, m % 2, :]).then_inc(h1_highs, 1)

            def take_layer2(i, blocks=range(L2_BLOCKS)):
                for m in blocks:
                    act.wait_ge(out_ready[m], out_count(i, m, "l2", 1))
                    nc.scalar.activation(h2[:, m, :], p_out[:, m, 0:CHUNK], ACT.Relu,
                                         bias=b2s[:, m:m + 1]).then_inc(out_taken[m], 1)

            def take_layer3(i):
                act.wait_ge(out_ready[1], out_count(i, 1, "l3", 1))
                copy(y, p_out[0:1, 1, 0:CHUNK]).then_inc(out_taken[1], 1)
                act.wait_ge(out_taken[1], out_count(i, 1, "l3", 1))
                act.dma_start(out[:, bass.ds((i - 1) * CHUNK, CHUNK)], y).then_inc(y_stored, 16)

            def step(i, layers=True, last=False):
                for n in range(HALF):
                    take_transposes(i, 0, [2 * n + 1] if layers else [2 * n, 2 * n + 1])
                    take_picked(i, PICKED_AFTER[n])
                if layers:
                    take_layer1(i)
                else:
                    load_raw(3)
                    load_raw(4)
                take_gram(i, 0)
                if not layers:
                    cut_weights([3])
                for n in range(HALF):
                    take_transposes(i, 1, [2 * n + 1] if layers else [2 * n, 2 * n + 1])
                    if layers and n < L2_BLOCKS:
                        take_layer2(i, [n])
                if layers:
                    take_layer3(i)
                else:
                    cut_weights([4])
                    load_raw(5)
                take_gram(i, 1)
                if not last:
                    take_picked(i + 1, PICKED_AHEAD)
                if layers:
                    act.wait_ge(y_stored, 16 * i)
                else:
                    cut_weights([5])

            act.wait_ge(tab_lows, N)
            take_picked(0, PICKED_AHEAD[:1])
            act.wait_ge(side_loaded, 16)
            cut_weights(range(0, 3))
            take_picked(0, PICKED_AHEAD[1:])
            step(0, layers=False)
            act.wait_ge(weights_loaded, 3 * 16)
            with act.Fori(1, CHUNKS - 1) as i:
                step(i)
            step(CHUNKS - 1, last=True)
            take_layer1(CHUNKS)
            take_layer2(CHUNKS)
            take_layer3(CHUNKS)
            act.wait_ge(y_stored, 16 * CHUNKS)

        @block.vector
        def _(dve):
            copy = nc.vector.tensor_copy

            def make_onehots(i, half, tables):
                dve.wait_ge(ids_loaded[half], 16 * len(HALVES[half]) * (i + 1))
                for u in tables:
                    if not (isinstance(i, int) and i == 0 and half == 0):
                        chunk, before = (i, u - ONEHOTS) if half else (i - 1, max(range(u, N, ONEHOTS)))
                        dve.wait_ge(out_ready[before % 2], out_count(chunk, before % 2, "pick", before // 2 + 1))
                    for k in range(PICK_PER_PART):
                        last = nc.vector.tensor_scalar(onehot[:, u % ONEHOTS, k, :], ids32[:, u, :],
                                                       row_id[:, k:k + 1], None, ALU.is_equal)
                    last.then_inc(onehot_ready, 1)

            def cut_lows(i, c):
                at = slice(c * P, (c + 1) * P)
                dve.wait_ge(highs_cut, 3 * (TILES_PER_CHUNK * i + c) + 1)
                nc.vector.tensor_tensor(dense_low[:, at], xt[:, c, :, 0], dense_high[:, at].bitcast(fp32),
                                        ALU.subtract).then_inc(lows_cut, 1)
                dve.wait_ge(highs_cut, 3 * (TILES_PER_CHUNK * i + c) + 3)
                nc.vector.tensor_tensor(pairs_low[:, :, at], pairs[:], pairs_high[:, :, at].bitcast(fp32),
                                        ALU.subtract).then_inc(lows_cut, 1)

            def take_transposes(i, c, groups):
                for g in groups:
                    dve.wait_ge(transposed[0], tr_count(i, c, g) + 1)
                    copy_group(copy, c, g, tr_taken[0])

            def take_gram(i, c, groups=range(GRAM_GROUPS)):
                if 0 in groups:
                    wait(dve, highs_cut, 3 * (TILES_PER_CHUNK * i + c))
                for k in groups:
                    dve.wait_ge(gram_ready, gram_count(i, c, k + 1))
                    copy_gram(copy, k, (2, 3), gram_taken["dve"])

            def cut_h1(i, m):
                dve.wait_ge(h1_highs, L1_BLOCKS * (i - 1) + m + 1)
                nc.vector.tensor_tensor(h1_low[:, m, :], h1[:, m % 2, :], h1_high[:, m, :].bitcast(fp32),
                                        ALU.subtract).then_inc(h1_lows, 1)

            def first_step():
                for u in HALVES[1]:
                    make_onehots(0, 1, [u])
                cut_weights(range(0, 3))
                dve.wait_ge(w_lows, 1)
                nc.vector.memset(pairs[:, slots_of(BLOCKS - 1):, :], 0.0).then_inc(zeroed, 1)
                make_onehots(1, 0, HALVES[0])
                cut_lows(0, 0)
                cut_weights([3])
                make_onehots(1, 1, HALVES[1][:1])
                cut_weights([4])
                make_onehots(1, 1, HALVES[1][1:2])
                take_gram(0, 1)
                cut_weights([5])

            def step(i, last=False):
                take_transposes(i, 0, [0])
                make_onehots(i, 1, HALVES[1][2:])
                take_transposes(i, 0, range(2, NG, 2))
                cut_lows(i - 1, 1)
                for m in range(L1_BLOCKS):
                    if not last and m < ONEHOTS:
                        make_onehots(i + 1, 0, [m])
                    cut_h1(i, m)
                take_gram(i, 0)
                take_transposes(i, 1, [0])
                dve.wait_ge(out_ready[1], out_count(i, 1, "l1", L1_USES))
                cut_lows(i, 0)
                take_transposes(i, 1, range(2, NG, 2))
                if not last:
                    make_onehots(i + 1, 1, HALVES[1][:2])
                take_gram(i, 1)

            def cut_table(u):
                dve.wait_ge(tab_highs, u + 1)
                nc.vector.tensor_tensor(tab_low[:, u, :, :].rearrange("p k d -> p (k d)"), tab_raw[:, u, :],
                                        tab_high[:, u, :, :].rearrange("p k d -> p (k d)").bitcast(fp32),
                                        ALU.subtract).then_inc(tab_lows, 1)

            def cut_weights(cuts):
                for n in cuts:
                    if n < len(PAIR_CUTS):
                        dve.wait_ge(w_highs, n + 1)
                        for k, w in pair_cut(n):
                            last = nc.vector.scalar_tensor_tensor(wp[:, k, :], w, side[:, 1, k:k + 1],
                                                                  wp[:, k, :].bitcast(fp32), ALU.mult, ALU.add)
                        last.then_inc(w_lows, 1)
                        continue
                    held, _, width, high, low = CUTS[n]
                    whole = raw[held][:, 0:width]
                    if n == DENSE_CUT:
                        dve.wait_ge(raw_loaded[n], 16)
                        nc.vector.tensor_tensor(wd_sum, whole[:, 0:HIDDEN1], whole[:, HIDDEN1:], ALU.add
                                                ).then_inc(wd_added, 1)
                        whole = wd_sum
                    dve.wait_ge(w_highs, n + 1)
                    nc.vector.tensor_tensor(low, whole, high.bitcast(fp32), ALU.subtract).then_inc(w_lows, 1)

            for u in range(2):
                cut_table(u)
            dve.wait_ge(row_id_loaded, 16)
            make_onehots(0, 0, [0])
            for u in range(2, N):
                cut_table(u)
            make_onehots(0, 0, range(1, ONEHOTS))
            dve.wait_ge(tab_lows, N)
            nc.vector.memset(xt[:, :, :, DENSE_AGAIN + 1:], 0.0).then_inc(zeroed, 1)
            first_step()
            with dve.Fori(1, CHUNKS - 1) as i:
                step(i)
            step(CHUNKS - 1, last=True)
            cut_lows(CHUNKS - 1, 1)
            for m in range(L1_BLOCKS):
                cut_h1(CHUNKS, m)


def kernel(**inputs):
    import numpy as np
    import concourse.bacc as bacc
    from concourse import mybir as _mybir
    from concourse.bass_utils import run_bass_kernel_spmd

    nc = bacc.Bacc("TRN2", target_bir_lowering=False, num_devices=1)
    arrays = {}

    def give(name, a):
        a = np.ascontiguousarray(a)
        arrays[name] = a
        return nc.dram_tensor(name, a.shape, _mybir.dt.from_np(a.dtype), kind="ExternalInput").ap()

    ids = np.asarray(inputs["ids"])
    w1 = np.asarray(inputs["W_top1"])
    n_pairs = FEATURES * (FEATURES - 1) // 2
    w_pairs = np.zeros((BLOCKS, 32, SLOTS, HIDDEN1), w1.dtype)
    sides = np.zeros((BLOCKS, 32, 2, SLOTS), np.float32)
    for b in range(1, FEATURES):
        j, slot = (b - 1) // SLOTS, (b - 1) % SLOTS
        for row in range(DENSE_AGAIN + 1):
            a = 0 if row == DENSE_AGAIN else row
            if row == b:
                continue
            f, g = sorted((ORDER[a], ORDER[b]))
            w_pairs[j, row, slot] = w1[DIM + f * FEATURES - f * (f + 1) // 2 + g - f - 1]
            sides[j, row, :, slot] = (1, 0) if row < b else (-1, 1)
    w_dense = np.stack([w1[:DIM], w1[DIM + n_pairs:]], axis=1)
    out = nc.dram_tensor("y_out", (BATCH, 1), _mybir.dt.from_np(w1.dtype), kind="ExternalOutput").ap()
    build(
        nc,
        dense=give("dense", inputs["r_dense_features"]),
        ids=give("ids", ids),
        ids_rows=give("ids_rows", ids.T),
        tables=[give(f"tbl_{f}", inputs[f"tbl_{f}"]) for f in range(NUM_TABLES)],
        w_pairs=give("w_pairs", w_pairs.reshape(P, SLOTS, HIDDEN1)),
        w_dense=give("w_dense", w_dense.reshape(P, 2 * HIDDEN1)),
        b1=give("b1", np.asarray(inputs["b_top1"]).reshape(L1_BLOCKS, P).T),
        w2=give("w2", np.asarray(inputs["W_top2"]).reshape(L1_BLOCKS, P, HIDDEN2).transpose(1, 0, 2)
                .reshape(P, L1_BLOCKS * HIDDEN2)),
        b2=give("b2", np.asarray(inputs["b_top2"]).reshape(L2_BLOCKS, P).T),
        w3=give("w3", np.asarray(inputs["W_top3"]).reshape(L2_BLOCKS, P).T),
        identity=give("identity", np.eye(P, dtype=np.float32)),
        row_ids=give("row_ids", np.arange(PICK_ROWS, dtype=np.float32).reshape(PICK_PARTS, PICK_PER_PART)),
        sides=give("sides", sides.reshape(P, 2, SLOTS)),
        out=out.rearrange("b o -> o b"),
    )
    r = run_bass_kernel_spmd(nc, [arrays], core_ids=[0])
    return r.results[0]["y_out"]
```
